# Optimizing a Trainium2 kernel written in Bass

```python
import numpy as np
import jax
import jax.numpy as jnp

def _softmax(x, axis=-1):
    return jax.nn.softmax(x, axis=axis)

def _gelu(x):
    return jax.nn.gelu(x, approximate=True)

def _silu(x):
    return jax.nn.silu(x)

def _sigmoid(x):
    return jax.nn.sigmoid(x)

def _layernorm(x, axis=-1, eps=1e-05):
    m = jnp.mean(x, axis=axis, keepdims=True)
    v = jnp.var(x, axis=axis, keepdims=True)
    return (x - m) / jnp.sqrt(v + eps)

def _scatter_add(tgt, idx, src, axis=0):
    return tgt.at[idx].add(src)

def _segment_sum(src, seg, n):
    return jax.ops.segment_sum(src, seg, n)
kernel_name = 'mk_dlrm_tower_d1_rec_r8_1448eb'

def setup_inputs(seed: int=0):
    np.random.seed(seed)
    _w = jnp.asarray

    def _rec_inputs():
        import jax
        import jax.numpy as jnp
        _tk = jax.random.key(seed)
        ids = jnp.stack([jax.random.randint(jax.random.fold_in(_tk, 200 + f), (512,), 0, v, jnp.int32) for f, v in enumerate([12500, 125000, 12500, 12500, 12500, 1250, 1000, 12500, 1250, 12500, 1000, 1000, 1000, 12500, 1250, 12500, 1250, 12500, 1000, 1000, 1000, 1000, 1000, 1000, 1000, 1000])], axis=1)
        tbl_0 = 0.05 * jax.random.normal(jax.random.fold_in(_tk, 500 + 0), (12500, 128), jnp.float32)
        tbl_1 = 0.05 * jax.random.normal(jax.random.fold_in(_tk, 500 + 1), (125000, 128), jnp.float32)
        tbl_2 = 0.05 * jax.random.normal(jax.random.fold_in(_tk, 500 + 2), (12500, 128), jnp.float32)
        tbl_3 = 0.05 * jax.random.normal(jax.random.fold_in(_tk, 500 + 3), (12500, 128), jnp.float32)
        tbl_4 = 0.05 * jax.random.normal(jax.random.fold_in(_tk, 500 + 4), (12500, 128), jnp.float32)
        tbl_5 = 0.05 * jax.random.normal(jax.random.fold_in(_tk, 500 + 5), (1250, 128), jnp.float32)
        tbl_6 = 0.05 * jax.random.normal(jax.random.fold_in(_tk, 500 + 6), (1000, 128), jnp.float32)
        tbl_7 = 0.05 * jax.random.normal(jax.random.fold_in(_tk, 500 + 7), (12500, 128), jnp.float32)
        tbl_8 = 0.05 * jax.random.normal(jax.random.fold_in(_tk, 500 + 8), (1250, 128), jnp.float32)
        tbl_9 = 0.05 * jax.random.normal(jax.random.fold_in(_tk, 500 + 9), (12500, 128), jnp.float32)
        tbl_10 = 0.05 * jax.random.normal(jax.random.fold_in(_tk, 500 + 10), (1000, 128), jnp.float32)
        tbl_11 = 0.05 * jax.random.normal(jax.random.fold_in(_tk, 500 + 11), (1000, 128), jnp.float32)
        tbl_12 = 0.05 * jax.random.normal(jax.random.fold_in(_tk, 500 + 12), (1000, 128), jnp.float32)
        tbl_13 = 0.05 * jax.random.normal(jax.random.fold_in(_tk, 500 + 13), (12500, 128), jnp.float32)
        tbl_14 = 0.05 * jax.random.normal(jax.random.fold_in(_tk, 500 + 14), (1250, 128), jnp.float32)
        tbl_15 = 0.05 * jax.random.normal(jax.random.fold_in(_tk, 500 + 15), (12500, 128), jnp.float32)
        tbl_16 = 0.05 * jax.random.normal(jax.random.fold_in(_tk, 500 + 16), (1250, 128), jnp.float32)
        tbl_17 = 0.05 * jax.random.normal(jax.random.fold_in(_tk, 500 + 17), (12500, 128), jnp.float32)
        tbl_18 = 0.05 * jax.random.normal(jax.random.fold_in(_tk, 500 + 18), (1000, 128), jnp.float32)
        tbl_19 = 0.05 * jax.random.normal(jax.random.fold_in(_tk, 500 + 19), (1000, 128), jnp.float32)
        tbl_20 = 0.05 * jax.random.normal(jax.random.fold_in(_tk, 500 + 20), (1000, 128), jnp.float32)
        tbl_21 = 0.05 * jax.random.normal(jax.random.fold_in(_tk, 500 + 21), (1000, 128), jnp.float32)
        tbl_22 = 0.05 * jax.random.normal(jax.random.fold_in(_tk, 500 + 22), (1000, 128), jnp.float32)
        tbl_23 = 0.05 * jax.random.normal(jax.random.fold_in(_tk, 500 + 23), (1000, 128), jnp.float32)
        tbl_24 = 0.05 * jax.random.normal(jax.random.fold_in(_tk, 500 + 24), (1000, 128), jnp.float32)
        tbl_25 = 0.05 * jax.random.normal(jax.random.fold_in(_tk, 500 + 25), (1000, 128), jnp.float32)
        _rk = jax.random.fold_in(_tk, 7)
        r_dense_features = -0.000520686 + 1.00062 * jax.random.normal(jax.random.fold_in(_rk, 101), (512, 128), jnp.float32)
        W_top1 = 0.0405887 * jax.random.normal(jax.random.fold_in(_tk, 801), (607, 512), jnp.float32)
        W_top2 = 0.0441942 * jax.random.normal(jax.random.fold_in(_tk, 802), (512, 256), jnp.float32)
        W_top3 = 0.0625 * jax.random.normal(jax.random.fold_in(_tk, 803), (256, 1), jnp.float32)
        b_top1 = jnp.zeros((512,), jnp.float32)
        b_top2 = jnp.zeros((256,), jnp.float32)
        return (r_dense_features, ids, tbl_0, tbl_1, tbl_2, tbl_3, tbl_4, tbl_5, tbl_6, tbl_7, tbl_8, tbl_9, tbl_10, tbl_11, tbl_12, tbl_13, tbl_14, tbl_15, tbl_16, tbl_17, tbl_18, tbl_19, tbl_20, tbl_21, tbl_22, tbl_23, tbl_24, tbl_25, W_top1, b_top1, W_top2, b_top2, W_top3)
    r_dense_features, ids, tbl_0, tbl_1, tbl_2, tbl_3, tbl_4, tbl_5, tbl_6, tbl_7, tbl_8, tbl_9, tbl_10, tbl_11, tbl_12, tbl_13, tbl_14, tbl_15, tbl_16, tbl_17, tbl_18, tbl_19, tbl_20, tbl_21, tbl_22, tbl_23, tbl_24, tbl_25, W_top1, b_top1, W_top2, b_top2, W_top3 = _rec_inputs()

    def _L0_rec_setup():
        import jax, jax.numpy as jnp
        import numpy as np
        NUM_SPARSE = 26
        EMBED_DIM = 128
        BATCH = 2048
        key = jax.random.key(seed)
        k1, k2 = jax.random.split(key)
        dense_features = jax.random.normal(k1, (BATCH, EMBED_DIM), dtype=jnp.float32)
        sparse_features = jax.random.normal(k2, (BATCH, NUM_SPARSE, EMBED_DIM), dtype=jnp.float32)
        return {'dense_features': dense_features, 'sparse_features': sparse_features}
    _L0_rec_all = _L0_rec_setup()
    _L0_rec_in = {k: v for k, v in _L0_rec_all.items() if k in ()}
    del _L0_rec_all
    return {'r_dense_features': r_dense_features, 'ids': ids, 'tbl_0': tbl_0, 'tbl_1': tbl_1, 'tbl_2': tbl_2, 'tbl_3': tbl_3, 'tbl_4': tbl_4, 'tbl_5': tbl_5, 'tbl_6': tbl_6, 'tbl_7': tbl_7, 'tbl_8': tbl_8, 'tbl_9': tbl_9, 'tbl_10': tbl_10, 'tbl_11': tbl_11, 'tbl_12': tbl_12, 'tbl_13': tbl_13, 'tbl_14': tbl_14, 'tbl_15': tbl_15, 'tbl_16': tbl_16, 'tbl_17': tbl_17, 'tbl_18': tbl_18, 'tbl_19': tbl_19, 'tbl_20': tbl_20, 'tbl_21': tbl_21, 'tbl_22': tbl_22, 'tbl_23': tbl_23, 'tbl_24': tbl_24, 'tbl_25': tbl_25, 'W_top1': W_top1, 'b_top1': b_top1, 'W_top2': W_top2, 'b_top2': b_top2, 'W_top3': W_top3}

def reference(r_dense_features, ids, tbl_0, tbl_1, tbl_2, tbl_3, tbl_4, tbl_5, tbl_6, tbl_7, tbl_8, tbl_9, tbl_10, tbl_11, tbl_12, tbl_13, tbl_14, tbl_15, tbl_16, tbl_17, tbl_18, tbl_19, tbl_20, tbl_21, tbl_22, tbl_23, tbl_24, tbl_25, W_top1, b_top1, W_top2, b_top2, W_top3):
    import jax
    import jax.numpy as jnp

    def _L0_rec_ref(dense_features, sparse_features):
        import jax, jax.numpy as jnp
        import numpy as np
        NUM_SPARSE = 26
        EMBED_DIM = 128
        BATCH = 2048
        F = NUM_SPARSE + 1
        combined = jnp.concatenate([dense_features[:, None, :], sparse_features], axis=1)
        interactions = jnp.einsum('bfd,bgd->bfg', combined, combined)
        iu, ju = jnp.triu_indices(F, k=1)
        interactions_flat = interactions[:, iu, ju]
        return jnp.concatenate([dense_features, interactions_flat], axis=1)
    e = jnp.stack([tbl_0[ids[:, 0]], tbl_1[ids[:, 1]], tbl_2[ids[:, 2]], tbl_3[ids[:, 3]], tbl_4[ids[:, 4]], tbl_5[ids[:, 5]], tbl_6[ids[:, 6]], tbl_7[ids[:, 7]], tbl_8[ids[:, 8]], tbl_9[ids[:, 9]], tbl_10[ids[:, 10]], tbl_11[ids[:, 11]], tbl_12[ids[:, 12]], tbl_13[ids[:, 13]], tbl_14[ids[:, 14]], tbl_15[ids[:, 15]], tbl_16[ids[:, 16]], tbl_17[ids[:, 17]], tbl_18[ids[:, 18]], tbl_19[ids[:, 19]], tbl_20[ids[:, 20]], tbl_21[ids[:, 21]], tbl_22[ids[:, 22]], tbl_23[ids[:, 23]], tbl_24[ids[:, 24]], tbl_25[ids[:, 25]]], axis=1)
    z = _L0_rec_ref(r_dense_features, e)
    z = z.reshape(z.shape[0], -1)
    h = jnp.concatenate([z, r_dense_features], axis=1)
    h = jnp.maximum(h @ W_top1 + b_top1, 0.0)
    h = jnp.maximum(h @ W_top2 + b_top2, 0.0)
    y = h @ W_top3
    return y

_drawn_inputs = setup_inputs


def setup_inputs(seed=0):
    import zlib

    import numpy as np

    out = dict(_drawn_inputs(seed))
    spreads = {'b_top1': (0.0, 0.1), 'b_top2': (0.0, 0.1)}
    factors = {}
    for name, (base, spread) in spreads.items():
        noise = np.random.default_rng([zlib.crc32(name.encode()), seed]).standard_normal(out[name].shape)
        drawn = base * np.exp(spread * noise) if base else spread * noise
        out[name] = jnp.asarray(drawn.astype(out[name].dtype))
    for name, factor in factors.items():
        out[name] = (out[name] * factor).astype(out[name].dtype)
    return out
```

```python
from contextlib import ExitStack

import concourse.bass as bass
from concourse import mybir

F32 = mybir.dt.float32
BF16 = mybir.dt.bfloat16
I32 = mybir.dt.int32
I16 = mybir.dt.int16
ALU = mybir.AluOpType
ACT = mybir.ActivationFunctionType

P = 128
BATCH = 512
EMB = 128
TABLES = 26
FEATS = TABLES + 1
SLOTS = 32
TILES = BATCH // P
QUADS = P // SLOTS
GROUPS = P // QUADS

PICKED = 8
GATHERED = TABLES - PICKED
PICK_ROWS = 1000
EMB_TILES = 3
COL_RING = 4
RING = 3
CHUNKS = 8
PR = PICK_ROWS // CHUNKS
PR16 = PR // 16 * 16

TURN = 4
TURNS = [(f, min(f + TURN, GATHERED + 1)) for f in range(0, GATHERED + 1, TURN)]
NT = len(TURNS)

RB = 3
BLOCKS = FEATS // RB
BLOCK_LEN = [FEATS - 1 - RB * k for k in range(BLOCKS)]
BLOCK_AT = [RB * sum(BLOCK_LEN[:k]) for k in range(BLOCKS)]
PAIRS = BLOCK_AT[-1] + RB * BLOCK_LEN[-1]
KC = -(-PAIRS // P)
H1 = 512
H2 = 256
N1 = H1 // P
N2 = H2 // P
GRAM_HALF = GROUPS // 2

PICK_TURNS = [0, 1, 2, 3, 4, 5, 7, 8]
TILE_TURNS = [
    {"gram0": 10, "gram1": 10, "rows": 11, "cols": 12, "layer1": 12, "layer2": 12},
    {"gram0": 12, "gram1": 13, "rows": 14, "cols": 15, "layer1": 15, "layer2": 15},
    {"gram0": 15, "gram1": 16, "rows": 17, "cols": 18, "layer1": 19, "layer2": 19},
    {"gram0": 20, "gram1": 20, "rows": 20, "cols": 20, "layer1": 20, "layer2": 20},
]


def dlrm_program(nc, dense, ids_rows, ids_cols, tables, w1, w2, small, out):
    with ExitStack() as ctx:
        def sb(name, shape, dt):
            return ctx.enter_context(nc.sbuf_tensor(name, shape, dt))

        def bank(name):
            return ctx.enter_context(nc.psum_tensor(name, [P, 512], F32))

        def sem(name):
            return ctx.enter_context(nc.semaphore(name))

        row_ids = sb("row_ids", [P, TILES, TABLES], I32)
        col_ids = sb("col_ids", [P, COL_RING, BATCH], I32)
        col_ids16 = sb("col_ids16", [P, COL_RING, BATCH], I16)
        chunk_row = sb("chunk_row", [P, CHUNKS], I32)
        chunk_rows = sb("chunk_rows", [P, CHUNKS, BATCH], I16)
        dense_sb = sb("dense_sb", [P, TILES, EMB], F32)
        emb = sb("emb", [P, EMB_TILES, GATHERED, EMB], F32)
        embT = sb("embT", [P, BATCH, SLOTS], F32)
        denseT = sb("denseT", [P, BATCH], F32)
        ident = sb("ident", [P, P], F32)
        ones = sb("ones", [P, P], F32)
        table = sb("table", [P, RING, CHUNKS, EMB], F32)
        rest = sb("rest", [P, 2, CHUNKS, EMB], F32)
        last_part = sb("last_part", [P, 2, CHUNKS, EMB], BF16)
        one_hot = sb("one_hot", [P, 2, CHUNKS, BATCH], BF16)
        dots = sb("dots", [P, 2, FEATS, GROUPS], F32)
        pairs = sb("pairs", [GROUPS, 2, QUADS, KC * P], F32)
        pairsT = sb("pairsT", [P, KC, P], F32)
        w1_sb = sb("w1_sb", [P, KC + 2, H1], F32)
        w1_dense = sb("w1_dense", [P, H1], F32)
        w2_sb = sb("w2_sb", [P, N1, H2], F32)
        small_sb = sb("small_sb", [P, N1 + N2 + N2], F32)
        h1 = sb("h1", [P, N1, P], F32)
        h2 = sb("h2", [P, N2, P], F32)
        y_sb = sb("y_sb", [1, BATCH], F32)
        b1 = small_sb[:, 0:N1]
        b2 = small_sb[:, N1:N1 + N2]
        w3 = small_sb[:, N1 + N2:N1 + 2 * N2]

        turn_ps = [bank("turn_ps0"), bank("turn_ps1")]
        pick_ps = [bank("pick_ps0"), bank("pick_ps1")]
        gram_ps = [bank("gram_ps0"), bank("gram_ps1")]
        row_ps = [bank("row_ps0"), bank("row_ps1")]
        layer1_ps = pick_ps
        y_ps = pick_ps[0]
        cols_ps = row_ps[0]
        layer2_ps = [row_ps[1], row_ps[0]]

        row_ids_in = sem("row_ids_in")
        col_ids_in = [sem(f"col_ids_in{j}") for j in range(PICKED)]
        dense_in = sem("dense_in")
        weights_in = sem("weights_in")
        table_in = [sem(f"table_in{j}") for j in range(PICKED)]
        rows_in = [[sem(f"rows_in{t}_{k}") for k in range(NT)] for t in range(TILES)]
        out_stored = sem("out_stored")
        ones_set = sem("ones_set")
        ident_set = sem("ident_set")
        chunk_row_set = sem("chunk_row_set")
        chunk_rows_set = sem("chunk_rows_set")
        ids16_set = sem("ids16_set")
        pads_set = sem("pads_set")
        w1_dense_set = sem("w1_dense_set")
        rest_set = sem("rest_set")
        parts_set = sem("parts_set")
        one_hot_set = sem("one_hot_set")
        picked = sem("picked")
        picked_out = sem("picked_out")
        turned = sem("turned")
        turned_out = sem("turned_out")
        gram_done = sem("gram_done")
        gram_out = sem("gram_out")
        rows_done = sem("rows_done")
        rows_out = [sem("rows_out_dve"), sem("rows_out_act")]
        cols_done = sem("cols_done")
        cols_out = sem("cols_out")
        layer1_done = sem("layer1_done")
        layer1_out = [sem("layer1_out_act"), sem("layer1_out_dve")]
        layer2_done = sem("layer2_done")
        layer2_out = [sem("layer2_out_act"), sem("layer2_out_dve")]
        y_done = sem("y_done")
        y_out = sem("y_out")

        even_blocks = (BLOCKS + 1) // 2
        odd_blocks = BLOCKS // 2

        def blocks_out(t, k):
            return t * (even_blocks if k % 2 == 0 else odd_blocks) + k // 2 + 1

        def row_block_views(t, k):
            n, at = BLOCK_LEN[k], BLOCK_AT[k]
            src = row_ps[k % 2][0:GROUPS, 0:RB * P].rearrange("p (r q f) -> p r q f", r=RB, q=QUADS)
            dst = pairs[:, t % 2, :, at:at + RB * n].rearrange("p q (r c) -> p r q c", r=RB)
            return dst, src[:, :, :, FEATS - n:FEATS]

        def upper_half(x):
            return x.bitcast(BF16).rearrange("p c (d e) -> p c d e", e=2)[:, :, :, 1]

        block = ctx.enter_context(nc.Block())

        @block.sync
        def _(sp):
            sp.dma_start(row_ids[:], ids_rows).then_inc(row_ids_in, 16)
            for j in range(PICKED):
                if j >= RING:
                    sp.wait_ge(picked, j - RING + 1)
                if j >= COL_RING:
                    sp.wait_ge(ids16_set, j - COL_RING + 1)
                sp.dma_start(col_ids[:, j % COL_RING], ids_cols[:, j]).then_inc(col_ids_in[j], 16)
                rows = tables[GATHERED + j].rearrange("(p c) d -> p c d", c=CHUNKS)
                sp.dma_start(table[0:PR16, j % RING], rows[0:PR16]).then_inc(table_in[j], 16)
                sp.dma_start(table[PR16:PR, j % RING], rows[PR16:PR]).then_inc(table_in[j], 16)
                if j == 0:
                    sp.dma_start(dense_sb[:], dense).then_inc(dense_in, 16)
                if j == RING - 1:
                    sp.dma_start(w1_sb[:], w1).then_inc(weights_in, 16)
                    sp.dma_start(w2_sb[:], w2).then_inc(weights_in, 16)
                    sp.dma_start(small_sb[:], small).then_inc(weights_in, 16)
            sp.wait_ge(y_out, TILES)
            sp.dma_start(out, y_sb[:]).then_inc(out_stored, 16)
            sp.wait_ge(out_stored, 16)

        @block.gpsimd
        def _(pool):
            nc.gpsimd.iota(chunk_row[:], [[1, CHUNKS]], base=0, channel_multiplier=CHUNKS).then_inc(chunk_row_set, 1)
            pool.wait_ge(ones_set, 1)
            nc.gpsimd.affine_select(out=ident[:], in_=ones[:], compare_op=ALU.is_equal, fill=0.0, base=0,
                                    pattern=[[-1, P]], channel_multiplier=1).then_inc(ident_set, 1)
            pool.wait_ge(row_ids_in, 16)
            for t in range(TILES):
                for k, (f0, f1) in enumerate(TURNS):
                    if t >= EMB_TILES:
                        pool.wait_ge(turned, (t - EMB_TILES) * NT + k + 1)
                    for f in range(max(f0, 1), f1):
                        pool.indirect_dma_start(
                            emb[:, t % EMB_TILES, f - 1], None, tables[f - 1],
                            bass.IndirectOffsetOnAxis(ap=row_ids[:, t, f - 1:f], axis=0)).then_inc(rows_in[t][k], 16)

        @block.tensor
        def _(pe):
            turns_made = 0

            def turn_until(n):
                nonlocal turns_made
                while turns_made < n:
                    x = turns_made
                    t, k = x // NT, x % NT
                    f0, f1 = TURNS[k]
                    if x == 0:
                        pe.wait_ge(ident_set, 1)
                        pe.wait_ge(dense_in, 16)
                    pe.wait_ge(rows_in[t][k], 16 * (f1 - max(f0, 1)))
                    if x >= 2:
                        pe.wait_ge(turned_out, x - 1)
                    for f in range(f0, f1):
                        rows = dense_sb[:, t] if f == 0 else emb[:, t % EMB_TILES, f - 1]
                        mm = pe.transpose(turn_ps[x % 2][:, (f - f0) * P:(f - f0 + 1) * P], rows, ident[:])
                    mm.then_inc(turned, 1)
                    turns_made += 1

            for j in range(PICKED):
                turn_until(PICK_TURNS[j])
                pe.wait_ge(table_in[j], 32)
                pe.wait_ge(one_hot_set, j + 1)
                if j >= 2:
                    pe.wait_ge(picked_out, j - 1)
                parts = [upper_half(table[0:PR, j % RING]), upper_half(rest[0:PR, j % 2]), last_part[0:PR, j % 2]]
                for n, part in enumerate(parts):
                    if n == 1:
                        pe.wait_ge(parts_set, j + 1)
                    for c in range(CHUNKS):
                        mm = pe.matmul(pick_ps[j % 2][:], part[:, c], one_hot[0:PR, j % 2, c],
                                       start=(n == 0 and c == 0), stop=(n == 2 and c == CHUNKS - 1))
                mm.then_inc(picked, 1)

            for t in range(TILES):
                due = TILE_TURNS[t]
                for half in range(2):
                    turn_until(due[f"gram{half}"])
                    if half == 0:
                        pe.wait_ge(turned_out, (t + 1) * NT)
                        if t == 0:
                            pe.wait_ge(picked_out, PICKED)
                            pe.wait_ge(pads_set, 2)
                    if t >= 1:
                        pe.wait_ge(gram_out, 2 * (t - 1) + half + 1)
                    for g in range(GRAM_HALF):
                        for q in range(QUADS):
                            b = t * P + q * GROUPS + half * GRAM_HALF + g
                            mm = pe.matmul(gram_ps[half][q * SLOTS:(q + 1) * SLOTS, g * FEATS:(g + 1) * FEATS],
                                           embT[:, b, :], embT[:, b, 0:FEATS], start=True, stop=True,
                                           tile_position=(0, q * SLOTS))
                    mm.then_inc(gram_done, 1)

                turn_until(due["rows"])
                pe.wait_ge(gram_out, 2 * (t + 1))
                if t >= 1:
                    pe.wait_ge(y_out, t)
                for k in range(BLOCKS):
                    if k >= 2:
                        pe.wait_ge(rows_out[k % 2], blocks_out(t, k - 2))
                    for r in range(RB):
                        mm = pe.transpose(row_ps[k % 2][0:GROUPS, r * P:(r + 1) * P],
                                          dots[:, t % 2, RB * k + r, :], ident[:])
                    mm.then_inc(rows_done, 1)

                turn_until(due["cols"])
                pe.wait_ge(rows_out[0], blocks_out(t, BLOCKS - 1))
                pe.wait_ge(rows_out[1], blocks_out(t, BLOCKS - 2))
                if t == 0:
                    pe.wait_ge(pads_set, 3)
                for c in range(KC):
                    for q in range(QUADS):
                        at = c * P + q * GROUPS
                        mm = pe.transpose(cols_ps[:, at:at + GROUPS], pairs[:, t % 2, q, c * P:(c + 1) * P],
                                          ident[0:GROUPS, 0:GROUPS])
                mm.then_inc(cols_done, 1)

                turn_until(due["layer1"])
                if t == 0:
                    pe.wait_ge(w1_dense_set, 1)
                if t >= 1:
                    pe.wait_ge(y_out, t)
                for n in range(N1):
                    dst = layer1_ps[n // 2][:, (n % 2) * P:(n % 2 + 1) * P]
                    pe.matmul(dst, w1_dense[:, n * P:(n + 1) * P], denseT[:, t * P:(t + 1) * P], start=True, stop=False)
                    if n == 0:
                        pe.wait_ge(cols_out, t + 1)
                    for c in range(KC):
                        mm = pe.matmul(dst, w1_sb[:, 2 + c, n * P:(n + 1) * P], pairsT[:, c],
                                       start=False, stop=(c == KC - 1))
                    if n % 2 == 1:
                        mm.then_inc(layer1_done, 1)

                turn_until(due["layer2"])
                for n in range(N2):
                    for c in range(N1):
                        if n == 0 and c % 2 == 0:
                            pe.wait_ge(layer1_out[c // 2], 2 * (t + 1))
                        mm = pe.matmul(layer2_ps[n][:, 0:P], w2_sb[:, c, n * P:(n + 1) * P], h1[:, c],
                                       start=(c == 0), stop=(c == N1 - 1))
                    mm.then_inc(layer2_done, 1)

                for c in range(N2):
                    pe.wait_ge(layer2_out[c], t + 1)
                    mm = pe.matmul(y_ps[0:1, 0:P], w3[:, c:c + 1], h2[:, c], start=(c == 0), stop=(c == N2 - 1))
                mm.then_inc(y_done, 1)

        @block.scalar
        def _(act):
            turns_out = 0

            def turn_until(n):
                nonlocal turns_out
                while turns_out < n:
                    x = turns_out
                    t, k = x // NT, x % NT
                    f0, f1 = TURNS[k]
                    src = turn_ps[x % 2][:, 0:(f1 - f0) * P].rearrange("p (f b) -> p f b", f=f1 - f0)
                    act.wait_ge(turned, x + 1)
                    if f0 == 0:
                        nc.scalar.copy(denseT[:, t * P:(t + 1) * P], src[:, 0])
                    nc.scalar.copy(embT[:, t * P:(t + 1) * P, f0:f1].rearrange("p b f -> p f b"),
                                   src).then_inc(turned_out, 1)
                    turns_out += 1

            act.wait_ge(chunk_row_set, 1)
            nc.scalar.copy(chunk_rows[:], chunk_row[:].rearrange("p (c o) -> p c o", o=1)
                           .to_broadcast([P, CHUNKS, BATCH])).then_inc(chunk_rows_set, 1)

            def narrow_ids(j):
                act.wait_ge(col_ids_in[j], 16)
                if j >= COL_RING:
                    act.wait_ge(one_hot_set, j - COL_RING + 1)
                nc.scalar.copy(col_ids16[:, j % COL_RING], col_ids[:, j % COL_RING]).then_inc(ids16_set, 1)

            for j in range(COL_RING):
                narrow_ids(j)
            for j in range(PICKED):
                turn_until(PICK_TURNS[j])
                act.wait_ge(picked, j + 1)
                nc.scalar.copy(embT[:, :, GATHERED + 1 + j], pick_ps[j % 2][:]).then_inc(picked_out, 1)
                if j + COL_RING < PICKED:
                    narrow_ids(j + COL_RING)

            for t in range(TILES):
                due = TILE_TURNS[t]
                turn_until(due["gram0"])
                turn_until(due["gram1"])
                turn_until(due["rows"])
                if t >= 2:
                    act.wait_ge(cols_done, t - 1)
                for k in range(1, BLOCKS, 2):
                    act.wait_ge(rows_done, t * BLOCKS + k + 1)
                    dst, src = row_block_views(t, k)
                    nc.scalar.copy(dst, src).then_inc(rows_out[1], 1)
                turn_until(due["cols"])
                turn_until(due["layer1"])
                if t == 0:
                    act.wait_ge(weights_in, 48)
                act.wait_ge(layer1_done, 2 * t + 1)
                if t >= 1:
                    act.wait_ge(layer2_done, 2 * t)
                for n in range(2):
                    nc.scalar.activation(h1[:, n], layer1_ps[0][:, n * P:(n + 1) * P], ACT.Relu,
                                         bias=b1[:, n:n + 1]).then_inc(layer1_out[0], 1)
                turn_until(due["layer2"])
                act.wait_ge(layer2_done, 2 * t + 1)
                if t >= 1:
                    act.wait_ge(y_done, t)
                nc.scalar.activation(h2[:, 0], layer2_ps[0][:, 0:P], ACT.Relu,
                                     bias=b2[:, 0:1]).then_inc(layer2_out[0], 1)

        @block.vector
        def _(dve):
            nc.vector.memset(ones[:], 1.0).then_inc(ones_set, 1)
            nc.vector.memset(embT[:, 0:BATCH // 2, FEATS:SLOTS], 0.0).then_inc(pads_set, 1)
            nc.vector.memset(embT[:, BATCH // 2:BATCH, FEATS:SLOTS], 0.0).then_inc(pads_set, 1)
            nc.vector.memset(pairs[:, :, :, PAIRS:KC * P], 0.0).then_inc(pads_set, 1)

            for j in range(PICKED):
                dve.wait_ge(table_in[j], 32)
                if j >= 2:
                    dve.wait_ge(picked, j - 1)
                whole = table[0:PR, j % RING]
                nc.vector.tensor_tensor(rest[0:PR, j % 2], whole, upper_half(whole), ALU.subtract).then_inc(rest_set, 1)
                if j == 0:
                    dve.wait_ge(chunk_rows_set, 1)
                dve.wait_ge(ids16_set, j + 1)
                nc.vector.tensor_tensor(one_hot[0:PR, j % 2], chunk_rows[0:PR],
                                        col_ids16[0:PR, j % COL_RING:j % COL_RING + 1].to_broadcast([PR, CHUNKS, BATCH]),
                                        ALU.is_equal).then_inc(one_hot_set, 1)
                dve.wait_ge(rest_set, j + 1)
                left = rest[0:PR, j % 2]
                nc.vector.tensor_tensor(last_part[0:PR, j % 2], left, upper_half(left), ALU.subtract).then_inc(parts_set, 1)

            dve.wait_ge(weights_in, 48)
            nc.vector.tensor_tensor(w1_dense[:], w1_sb[:, 0], w1_sb[:, 1], ALU.add).then_inc(w1_dense_set, 1)

            for t in range(TILES):
                for half in range(2):
                    dve.wait_ge(gram_done, 2 * t + half + 1)
                    if t >= 2:
                        dve.wait_ge(rows_done, (t - 1) * BLOCKS)
                    src = gram_ps[half][:, 0:GRAM_HALF * FEATS].rearrange("p (g f) -> p g f", f=FEATS)
                    dst = dots[:, t % 2, :, half * GRAM_HALF:(half + 1) * GRAM_HALF].rearrange("p f g -> p g f")
                    nc.vector.tensor_copy(dst, src).then_inc(gram_out, 1)
                if t >= 2:
                    dve.wait_ge(cols_done, t - 1)
                for k in range(0, BLOCKS, 2):
                    dve.wait_ge(rows_done, t * BLOCKS + k + 1)
                    dst, src = row_block_views(t, k)
                    nc.vector.tensor_copy(dst, src).then_inc(rows_out[0], 1)
                dve.wait_ge(cols_done, t + 1)
                if t >= 1:
                    dve.wait_ge(layer1_done, 2 * t)
                nc.vector.tensor_copy(pairsT[:].rearrange("p c b -> p (c b)"), cols_ps[:, 0:KC * P]).then_inc(cols_out, 1)
                dve.wait_ge(layer1_done, 2 * (t + 1))
                for n in range(2, N1):
                    nc.vector.tensor_scalar(h1[:, n], layer1_ps[1][:, (n - 2) * P:(n - 1) * P], b1[:, n:n + 1], 0.0,
                                            ALU.add, ALU.max).then_inc(layer1_out[1], 1)
                dve.wait_ge(layer2_done, 2 * (t + 1))
                nc.vector.tensor_scalar(h2[:, 1], layer2_ps[1][:, 0:P], b2[:, 1:2], 0.0,
                                        ALU.add, ALU.max).then_inc(layer2_out[1], 1)
                dve.wait_ge(y_done, t + 1)
                nc.vector.tensor_copy(y_sb[0:1, t * P:(t + 1) * P], y_ps[0:1, 0:P]).then_inc(y_out, 1)


def kernel(**inputs):
    import numpy as np
    import concourse.bacc as bacc
    from concourse.bass_utils import run_bass_kernel_spmd

    nc = bacc.Bacc("TRN2", target_bir_lowering=False, num_devices=1)
    arrays = {}

    def dram(name, array):
        array = np.ascontiguousarray(array)
        arrays[name] = array
        return nc.dram_tensor(name, array.shape, mybir.dt.from_np(array.dtype), kind="ExternalInput").ap()

    ids = np.asarray(inputs["ids"])
    ids_rows = dram("ids_rows", ids.reshape(TILES, P, TABLES).transpose(1, 0, 2))
    ids_cols = dram("ids_cols", ids[:, GATHERED:].T.reshape(1, PICKED, BATCH)).to_broadcast([P, PICKED, BATCH])
    dense = dram("dense", inputs["r_dense_features"]).rearrange("(t p) d -> p t d", p=P)
    tables = [dram(f"tbl_{i}", inputs[f"tbl_{i}"]) for i in range(TABLES)]

    w_in = np.asarray(inputs["W_top1"])
    w_rows = np.zeros(((KC + 2) * P, H1), w_in.dtype)
    n_pairs = FEATS * (FEATS - 1) // 2
    w_rows[0:P] = w_in[0:EMB]
    w_rows[P:2 * P] = w_in[EMB + n_pairs:]
    at = EMB
    for i in range(FEATS - 1):
        k, r = i // RB, i % RB
        to = 2 * P + BLOCK_AT[k] + r * BLOCK_LEN[k] + r
        n = FEATS - 1 - i
        w_rows[to:to + n] = w_in[at:at + n]
        at += n
    w1 = dram("w1", w_rows.reshape(KC + 2, P, H1).transpose(1, 0, 2))
    w2 = dram("w2", np.asarray(inputs["W_top2"]).reshape(N1, P, H2).transpose(1, 0, 2))
    small = dram("small", np.concatenate([
        np.asarray(inputs["b_top1"]).reshape(N1, P).T,
        np.asarray(inputs["b_top2"]).reshape(N2, P).T,
        np.asarray(inputs["W_top3"]).reshape(N2, P).T], axis=1))
    y = nc.dram_tensor("y", (1, BATCH), F32, kind="ExternalOutput").ap()

    dlrm_program(nc, dense, ids_rows, ids_cols, tables, w1, w2, small, y)
    result = run_bass_kernel_spmd(nc, [arrays], core_ids=[0])
    return result.results[0]["y"].reshape(BATCH, 1)
```

```python
from contextlib import ExitStack

import concourse.bass as bass
from concourse import mybir

F32 = mybir.dt.float32
F32R = mybir.dt.float32r
I32 = mybir.dt.int32
ALU = mybir.AluOpType
ACT = mybir.ActivationFunctionType

P = 128
BATCH = 512
EMB = 128
TABLES = 26
FEATS = TABLES + 1
SLOTS = 32
TILES = BATCH // P
QUADS = P // SLOTS
GROUPS = P // QUADS

PICKED = 8
GATHERED = TABLES - PICKED
PICK_ROWS = 1000
EMB_TILES = 2
COL_RING = 2
RING = 2
CHUNKS = 8
DVE_HOT = 7
PR = PICK_ROWS // CHUNKS
PR16 = PR // 16 * 16

TURN = 4
TURNS = [(f, min(f + TURN, GATHERED + 1)) for f in range(1, GATHERED + 1, TURN)]
NT = len(TURNS)

PAIR_AT = [i * (FEATS - 1) - i * (i - 1) // 2 for i in range(FEATS)]
PAIRS = FEATS * (FEATS - 1) // 2
KC = -(-PAIRS // P)
KLAST = PAIRS - (KC - 1) * P
WEIGHT_LOADS = 6
H1 = 512
H2 = 256
N1 = H1 // P
N2 = H2 // P
GRAM_HALF = GROUPS // 2

DOT_ROWS = P // GROUPS
BANK_ROWS = DOT_ROWS * QUADS
FILLS = -(-FEATS // BANK_ROWS)

ORDER = [
    ("pick", 0), ("pick", 1), ("turn", 1), ("pick", 2), ("turn", 2), ("pick", 3), ("turn", 3), ("pick", 4),
    ("turn", 4), ("pick", 5), ("turn", 5), ("pick", 6), ("turn", 6), ("pick", 7), ("turn", 7), ("gram", 3),
    ("turn", 8), ("gram", 4), ("turn", 9), ("rows", 0), ("turn", 10), ("gram", 5), ("cols", 0), ("gram", 6),
    ("layer1", 1), ("turn", 11), ("layer1", 2), ("gram", 7), ("layer1", 3), ("gram", 8), ("layer1", 4),
    ("turn", 12), ("rows", 1), ("layer2", 0), ("turn", 13), ("cols", 1), ("layer3", 0), ("layer1", 6),
    ("turn", 14), ("layer1", 7), ("turn", 15), ("gram", 9), ("layer1", 8), ("gram", 12), ("turn", 17),
    ("rows", 2), ("layer2", 1), ("turn", 17), ("cols", 2), ("layer3", 1), ("layer1", 10), ("turn", 18),
    ("layer1", 12), ("turn", 20), ("gram", 16), ("rows", 3), ("layer2", 2), ("cols", 3), ("layer3", 2),
    ("layer1", 16), ("layer2", 3), ("layer3", 3),
]

def dlrm_program(nc, dense, ids_rows, ids_cols, tables, w1, w2, small, out):
    with ExitStack() as ctx:
        def sb(name, shape, dt):
            return ctx.enter_context(nc.sbuf_tensor(name, shape, dt))

        def bank(name):
            return ctx.enter_context(nc.psum_tensor(name, [P, 512], F32))

        def sem(name):
            return ctx.enter_context(nc.semaphore(name))

        row_ids = sb("row_ids", [P, TILES, TABLES], I32)
        col_ids = sb("col_ids", [P, COL_RING, BATCH], I32)
        chunk_row = sb("chunk_row", [P, CHUNKS], I32)
        chunk_row_f = sb("chunk_row_f", [P, CHUNKS], F32)
        dense_sb = sb("dense_sb", [P, TILES, EMB], F32)
        emb = sb("emb", [P, EMB_TILES, GATHERED, EMB], F32)
        embT = sb("embT", [P, BATCH, SLOTS], F32)
        denseT = sb("denseT", [P, BATCH], F32)
        ident = sb("ident", [P, P], F32)
        ones = sb("ones", [P, P], F32)
        table = sb("table", [P, RING, CHUNKS, EMB], F32)
        table_hi = sb("table_hi", [P, 2, CHUNKS, EMB], F32R)
        table_lo = sb("table_lo", [P, 2, CHUNKS, EMB], F32R)
        minus_row = sb("minus_row", [P, 1], F32)
        distance_sq = sb("distance_sq", [P, BATCH], F32)
        one_hot = sb("one_hot", [P, 2, CHUNKS, BATCH], F32R)
        dots_buf = [sb("dots_even", [P, FEATS, GROUPS], F32), sb("dots_odd", [P, FEATS, GROUPS], F32)]
        pairs = sb("pairs", [GROUPS, QUADS, PAIRS], F32)
        pairsT = sb("pairsT", [P, KC, P], F32)
        w1_sb = sb("w1_sb", [P, KC + 2, H1], F32)
        w1_dense = sb("w1_dense", [P, H1], F32)
        w2_sb = sb("w2_sb", [P, N1, H2], F32)
        small_sb = sb("small_sb", [P, N1 + N2 + N2], F32)
        h1 = sb("h1", [P, N1, P], F32)
        h2 = sb("h2", [P, N2, P], F32)
        y_sb = sb("y_sb", [P, TILES], F32)
        b1 = small_sb[:, 0:N1]
        b2 = small_sb[:, N1:N1 + N2]
        w3 = small_sb[:, N1 + N2:N1 + 2 * N2]

        turn_ps = [bank("turn_ps0"), bank("turn_ps1")]
        pick_ps = [bank("pick_ps0"), bank("pick_ps1")]
        gram_ps = [bank("gram_ps0"), bank("gram_ps1")]
        row_ps = [bank("row_ps0"), bank("row_ps1")]
        layer1_ps = pick_ps
        layer2_ps = pick_ps
        y_ps = pick_ps[0]

        row_ids_in = sem("row_ids_in")
        col_ids_in = [sem(f"col_ids_in{j}") for j in range(PICKED)]
        dense_in = sem("dense_in")
        weights_in = sem("weights_in")
        table_in = [sem(f"table_in{j}") for j in range(PICKED)]
        rows_in = [[sem(f"rows_in{t}_{k}") for k in range(NT)] for t in range(TILES)]
        out_stored = sem("out_stored")
        ones_set = sem("ones_set")
        ident_set = sem("ident_set")
        chunk_row_set = sem("chunk_row_set")
        chunk_row_f_set = sem("chunk_row_f_set")
        pads_set = [sem("pads_set_dve"), sem("pads_set_pool")]
        w1_dense_set = sem("w1_dense_set")
        hi_set = sem("hi_set")
        lo_set = sem("lo_set")
        hot_set = sem("hot_set")
        minus_row_set = sem("minus_row_set")
        distance_set = sem("distance_set")
        act_hot_set = sem("act_hot_set")
        picked = sem("picked")
        picked_out = sem("picked_out")
        dense_turned = sem("dense_turned")
        dense_out = sem("dense_out")
        turned = sem("turned")
        turned_out = sem("turned_out")
        gram_done = sem("gram_done")
        gram_out = sem("gram_out")
        rows_done = sem("rows_done")
        rows_out = [sem("rows_out_dve"), sem("rows_out_act")]
        cols_done = sem("cols_done")
        cols_out = [sem("cols_out_dve"), sem("cols_out_act")]
        layer1_done = sem("layer1_done")
        layer1_out = [sem("layer1_out_act"), sem("layer1_out_dve")]
        layer2_done = sem("layer2_done")
        layer2_out = [sem("layer2_out_act"), sem("layer2_out_dve")]
        y_done = sem("y_done")
        y_out = sem("y_out")

        def row_views(i):
            part, at = i % DOT_ROWS * GROUPS, i // DOT_ROWS % QUADS * P
            src = row_ps[i // BANK_ROWS % 2][part:part + GROUPS, at:at + P].rearrange("p (q f) -> p q f", q=QUADS)
            return pairs[:, :, PAIR_AT[i]:PAIR_AT[i] + FEATS - 1 - i], src[:, :, i + 1:FEATS]

        def row_share(engine, fill):
            rows = range(fill * BANK_ROWS, min((fill + 1) * BANK_ROWS, FEATS - 1))
            return [i for i in rows if i % DOT_ROWS * 2 // DOT_ROWS == engine]

        def col_views(c):
            k = P if c < KC - 1 else KLAST
            return pairsT[0:k, c], row_ps[c // 2][0:k, c % 2 * P:(c % 2 + 1) * P]

        block = ctx.enter_context(nc.Block())

        @block.sync
        def _(sp):
            sp.dma_start(row_ids[:], ids_rows).then_inc(row_ids_in, 16)
            for j in range(PICKED):
                if j >= COL_RING:
                    sp.wait_ge(hot_set, 2 * (j - COL_RING + 1))
                    sp.wait_ge(distance_set, j - COL_RING + 1)
                if j == 0:
                    sp.dma_start(dense_sb[:], dense).then_inc(dense_in, 16)
                sp.dma_start(col_ids[:, j % COL_RING], ids_cols[:, j]).then_inc(col_ids_in[j], 16)
                if j >= RING:
                    sp.wait_ge(lo_set, j - RING + 1)
                rows = tables[GATHERED + j].rearrange("(p c) d -> p c d", c=CHUNKS)
                sp.dma_start(table[0:PR16, j % RING], rows[0:PR16]).then_inc(table_in[j], 16)
                sp.dma_start(table[PR16:PR, j % RING], rows[PR16:PR]).then_inc(table_in[j], 16)
                if j == PICKED - 1:
                    sp.dma_start(w1_sb[:, 0], w1[0:EMB]).then_inc(weights_in, 16)
                    sp.dma_start(w1_sb[:, 1], w1[EMB + PAIRS:]).then_inc(weights_in, 16)
                    sp.dma_start(w1_sb[:, 2:KC + 1], w1[EMB:EMB + (KC - 1) * P].rearrange("(c p) n -> p c n", p=P))\
                        .then_inc(weights_in, 16)
                    sp.dma_start(w1_sb[0:KLAST, KC + 1], w1[EMB + (KC - 1) * P:EMB + PAIRS]).then_inc(weights_in, 16)
                    sp.dma_start(w2_sb[:], w2.rearrange("(c p) n -> p c n", p=P)).then_inc(weights_in, 16)
                    sp.dma_start(small_sb[:], small).then_inc(weights_in, 16)
            sp.wait_ge(y_out, TILES)
            sp.dma_start(out, y_sb[:]).then_inc(out_stored, 16)
            sp.wait_ge(out_stored, 16)

        @block.gpsimd
        def _(pool):
            nc.gpsimd.iota(chunk_row[:], [[1, CHUNKS]], base=0, channel_multiplier=CHUNKS).then_inc(chunk_row_set, 1)
            pool.wait_ge(ones_set, 1)
            nc.gpsimd.affine_select(out=ident[:], in_=ones[:], compare_op=ALU.is_equal, fill=0.0, base=0,
                                    pattern=[[-1, P]], channel_multiplier=1).then_inc(ident_set, 1)
            nc.gpsimd.memset(embT[:, BATCH // 2:BATCH, FEATS:SLOTS], 0.0).then_inc(pads_set[1], 1)
            pool.wait_ge(row_ids_in, 16)
            for t in range(TILES):
                for k, (f0, f1) in enumerate(TURNS):
                    if t >= EMB_TILES:
                        pool.wait_ge(turned, (t - EMB_TILES) * NT + k + 1)
                    for f in range(f0, f1):
                        pool.indirect_dma_start(
                            emb[:, t % EMB_TILES, f - 1], None, tables[f - 1],
                            bass.IndirectOffsetOnAxis(ap=row_ids[:, t, f - 1:f], axis=0)).then_inc(rows_in[t][k], 16)

        @block.tensor
        def _(pe):
            turns_made = 0

            def turn_until(n):
                nonlocal turns_made
                while turns_made < n:
                    x = turns_made
                    t, k = x // NT, x % NT
                    f0, f1 = TURNS[k]
                    pe.wait_ge(rows_in[t][k], 16 * (f1 - f0))
                    if x >= 2:
                        pe.wait_ge(turned_out, x - 1)
                    elif x == 0:
                        pe.wait_ge(dense_out, 2)
                    for f in range(f0, f1):
                        mm = pe.transpose(turn_ps[x % 2][:, (f - f0) * P:(f - f0 + 1) * P],
                                          emb[:, t % EMB_TILES, f - 1], ident[:])
                    mm.then_inc(turned, 1)
                    turns_made += 1

            pe.wait_ge(ident_set, 1)
            pe.wait_ge(dense_in, 16)
            for t in range(TILES):
                mm = pe.transpose(turn_ps[0][:, t * P:(t + 1) * P], dense_sb[:, t], ident[:])
            mm.then_inc(dense_turned, 1)

            def pick(j):
                pe.wait_ge(hi_set, j + 1)
                pe.wait_ge(hot_set, 2 * j + 1)
                if j >= 2:
                    pe.wait_ge(picked_out, j - 1)
                for n, part in enumerate([table_hi, table_lo]):
                    if n == 1:
                        pe.wait_ge(lo_set, j + 1)
                    for c in range(CHUNKS):
                        if n == 0 and c == DVE_HOT // 2:
                            pe.wait_ge(hot_set, 2 * j + 2)
                        if n == 0 and c == DVE_HOT:
                            pe.wait_ge(act_hot_set, j + 1)
                        mm = pe.matmul(pick_ps[j % 2][:], part[0:PR, j % 2, c], one_hot[0:PR, j % 2, c],
                                       start=(n == 0 and c == 0), stop=(n == 1 and c == CHUNKS - 1))
                mm.then_inc(picked, 1)

            quarters_made = 0

            def gram_until(n):
                nonlocal quarters_made
                while quarters_made < n:
                    t, quarter = quarters_made // 4, quarters_made % 4
                    half = quarter // 2
                    if quarter == 0:
                        pe.wait_ge(turned_out, (t + 1) * NT)
                        if t == 0:
                            pe.wait_ge(picked_out, PICKED)
                            pe.wait_ge(pads_set[0], 1)
                            pe.wait_ge(pads_set[1], 1)
                    if t >= 1 and quarter % 2 == 0:
                        pe.wait_ge(gram_out, 2 * (t - 1) + half + 1)
                    for g in range(quarter * GROUPS // 4, (quarter + 1) * GROUPS // 4):
                        at = g % GRAM_HALF * FEATS
                        for q in range(QUADS):
                            b = t * P + q * GROUPS + g
                            mm = pe.matmul(gram_ps[half][q * SLOTS:(q + 1) * SLOTS, at:at + FEATS],
                                           embT[:, b, :], embT[:, b, 0:FEATS], start=True, stop=True,
                                           tile_position=(0, q * SLOTS))
                    if quarter % 2 == 1:
                        mm.then_inc(gram_done, 1)
                    quarters_made += 1

            def rows(t):
                pe.wait_ge(gram_out, 2 * (t + 1))
                if t >= 1:
                    pe.wait_ge(cols_out[0], t)
                    pe.wait_ge(cols_out[1], t)
                dots = dots_buf[t % 2]
                for fill in range(FILLS):
                    if fill >= 2:
                        pe.wait_ge(rows_out[0], t * FILLS + fill - 1)
                        pe.wait_ge(rows_out[1], t * FILLS + fill - 1)
                    for n, i in enumerate(range(fill * BANK_ROWS, min((fill + 1) * BANK_ROWS, FEATS), DOT_ROWS)):
                        src = dots[:, i:min(i + DOT_ROWS, FEATS)].rearrange("p r g -> p (r g)")
                        mm = pe.transpose(row_ps[fill % 2][0:src.shape[1], n * P:(n + 1) * P], src, ident[:])
                    mm.then_inc(rows_done, 1)

            def cols(t):
                pe.wait_ge(rows_out[0], (t + 1) * FILLS)
                pe.wait_ge(rows_out[1], (t + 1) * FILLS)
                for c in range(KC):
                    k = P if c < KC - 1 else KLAST
                    for q in range(QUADS):
                        at = c % 2 * P + q * GROUPS
                        mm = pe.transpose(row_ps[c // 2][0:k, at:at + GROUPS], pairs[:, q, c * P:c * P + k],
                                          ident[0:GROUPS, 0:GROUPS])
                    if c != 0:
                        mm.then_inc(cols_done, 1)

            blocks_made = 0

            def layer1_until(n):
                nonlocal blocks_made
                while blocks_made < n:
                    t, block_of = blocks_made // N1, blocks_made % N1
                    if block_of == 0 and t == 0:
                        pe.wait_ge(w1_dense_set, 1)
                    if block_of == 0 and t >= 1:
                        pe.wait_ge(y_out, t)
                    dst = layer1_ps[block_of // 2][:, block_of % 2 * P:(block_of % 2 + 1) * P]
                    at = slice(block_of * P, (block_of + 1) * P)
                    pe.matmul(dst, w1_dense[:, at], denseT[:, t * P:(t + 1) * P], start=True, stop=False)
                    if block_of == 0:
                        pe.wait_ge(cols_out[0], t + 1)
                        pe.wait_ge(cols_out[1], t + 1)
                    for c in range(KC):
                        k = P if c < KC - 1 else KLAST
                        mm = pe.matmul(dst, w1_sb[0:k, 2 + c, at], pairsT[0:k, c], start=False, stop=(c == KC - 1))
                    if block_of % 2 == 1:
                        mm.then_inc(layer1_done, 1)
                    blocks_made += 1

            def layer2(t):
                for n in range(N2):
                    for c in range(N1):
                        if n == 0 and c % 2 == 0:
                            pe.wait_ge(layer1_out[c // 2], t + 1)
                        mm = pe.matmul(layer2_ps[n][:, 0:P], w2_sb[:, c, n * P:(n + 1) * P], h1[:, c],
                                       start=(c == 0), stop=(c == N1 - 1))
                    mm.then_inc(layer2_done, 1)

            def layer3(t):
                pe.wait_ge(layer2_out[0], t + 1)
                pe.wait_ge(layer2_out[1], t + 1)
                for c in range(N2):
                    mm = pe.matmul(y_ps[:, 0:1], h2[:, c], w3[:, c:c + 1], start=(c == 0), stop=(c == N2 - 1))
                mm.then_inc(y_done, 1)

            steps = {"pick": pick, "turn": turn_until, "gram": gram_until, "rows": rows, "cols": cols,
                     "layer1": layer1_until, "layer2": layer2, "layer3": layer3}
            for step, n in ORDER:
                steps[step](n)

        @block.scalar
        def _(act):
            turns_out = 0

            def turn_until(n):
                nonlocal turns_out
                while turns_out < n:
                    x = turns_out
                    t, k = x // NT, x % NT
                    f0, f1 = TURNS[k]
                    src = turn_ps[x % 2][:, 0:(f1 - f0) * P].rearrange("p (f b) -> p f b", f=f1 - f0)
                    act.wait_ge(turned, x + 1)
                    nc.scalar.copy(embT[:, t * P:(t + 1) * P, f0:f1].rearrange("p b f -> p f b"),
                                   src).then_inc(turned_out, 1)
                    turns_out += 1

            def round_table(j):
                act.wait_ge(table_in[j], 32)
                if j >= 2:
                    act.wait_ge(picked, j - 1)
                nc.scalar.copy(table_hi[0:PR, j % 2], table[0:PR, j % RING]).then_inc(hi_set, 1)

            def make_hot(j):
                act.wait_ge(col_ids_in[j], 16)
                if j >= 1:
                    act.wait_ge(act_hot_set, j)
                nc.scalar.activation(distance_sq[0:PR], col_ids[0:PR, j % COL_RING], ACT.Square,
                                     bias=minus_row[0:PR]).then_inc(distance_set, 1)
                act.wait_ge(distance_set, j + 1)
                nc.scalar.activation(one_hot[0:PR, j % 2, DVE_HOT], distance_sq[0:PR], ACT.Relu,
                                     bias=ones[0:PR, 0:1], scale=-1.0).then_inc(act_hot_set, 1)

            def pick(j):
                if j + 1 < PICKED:
                    round_table(j + 1)
                    make_hot(j + 1)
                act.wait_ge(picked, j + 1)
                nc.scalar.copy(embT[:, :, GATHERED + 1 + j], pick_ps[j % 2][:]).then_inc(picked_out, 1)

            def rows(t):
                if t >= 1:
                    act.wait_ge(cols_done, 2 * t)
                for fill in range(FILLS):
                    act.wait_ge(rows_done, t * FILLS + fill + 1)
                    for i in row_share(1, fill):
                        dst, src = row_views(i)
                        last = nc.scalar.copy(dst, src)
                    last.then_inc(rows_out[1], 1)

            def cols(t):
                act.wait_ge(cols_done, 2 * (t + 1))
                if t >= 1:
                    act.wait_ge(layer1_done, 2 * t)
                dst, src = col_views(KC - 1)
                nc.scalar.copy(dst, src).then_inc(cols_out[1], 1)

            layer1_moved = 0

            def layer1_until(n):
                nonlocal layer1_moved
                t = layer1_moved
                if n < t * N1 + N1 // 2:
                    return
                layer1_moved += 1
                if t == 0:
                    act.wait_ge(weights_in, 16 * WEIGHT_LOADS)
                act.wait_ge(layer1_done, 2 * t + 1)
                if t >= 1:
                    act.wait_ge(layer2_done, 2 * t)
                for n in range(2):
                    last = nc.scalar.activation(h1[:, n], layer1_ps[0][:, n * P:(n + 1) * P], ACT.Relu,
                                                bias=b1[:, n:n + 1])
                last.then_inc(layer1_out[0], 1)

            def layer2(t):
                act.wait_ge(layer2_done, 2 * t + 1)
                if t >= 1:
                    act.wait_ge(y_done, t)
                nc.scalar.activation(h2[:, 0], layer2_ps[0][:, 0:P], ACT.Relu,
                                     bias=b2[:, 0:1]).then_inc(layer2_out[0], 1)

            act.wait_ge(chunk_row_set, 1)
            nc.scalar.mul(minus_row[:], chunk_row[:, DVE_HOT:DVE_HOT + 1], -1.0).then_inc(minus_row_set, 1)
            act.wait_ge(minus_row_set, 1)
            act.wait_ge(ones_set, 1)
            round_table(0)
            make_hot(0)
            act.wait_ge(dense_turned, 1)
            nc.scalar.copy(denseT[:], turn_ps[0][:]).then_inc(dense_out, 1)
            nc.scalar.copy(embT[:, :, 0], turn_ps[0][:]).then_inc(dense_out, 1)
            steps = {"pick": pick, "turn": turn_until, "rows": rows, "cols": cols, "layer1": layer1_until,
                     "layer2": layer2}
            for step, n in ORDER:
                if step in steps:
                    steps[step](n)

        @block.vector
        def _(dve):
            nc.vector.memset(ones[:], 1.0).then_inc(ones_set, 1)
            nc.vector.memset(embT[:, 0:BATCH // 2, FEATS:SLOTS], 0.0).then_inc(pads_set[0], 1)
            dve.wait_ge(chunk_row_set, 1)
            nc.vector.tensor_copy(chunk_row_f[:], chunk_row[:]).then_inc(chunk_row_f_set, 1)
            dve.wait_ge(chunk_row_f_set, 1)

            for j in range(PICKED):
                dve.wait_ge(col_ids_in[j], 16)
                if j >= 2:
                    dve.wait_ge(picked, j - 1)
                for c in range(DVE_HOT):
                    hot = nc.vector.tensor_scalar(one_hot[0:PR, j % 2, c], col_ids[0:PR, j % COL_RING],
                                                  chunk_row_f[0:PR, c:c + 1], None, ALU.is_equal)
                    if c + 1 in (DVE_HOT // 2, DVE_HOT):
                        hot.then_inc(hot_set, 1)
                dve.wait_ge(hi_set, j + 1)
                nc.vector.tensor_tensor(table_lo[0:PR, j % 2], table[0:PR, j % RING],
                                        table_hi[0:PR, j % 2].bitcast(F32), ALU.subtract).then_inc(lo_set, 1)

            dve.wait_ge(weights_in, 16 * WEIGHT_LOADS)
            nc.vector.tensor_tensor(w1_dense[:], w1_sb[:, 0], w1_sb[:, 1], ALU.add).then_inc(w1_dense_set, 1)

            halves_out = 0

            def gram_until(quarters):
                nonlocal halves_out
                while halves_out < quarters // 2:
                    t, half = halves_out // 2, halves_out % 2
                    dve.wait_ge(gram_done, halves_out + 1)
                    if t >= 2:
                        dve.wait_ge(rows_done, (t - 1) * FILLS)
                    src = gram_ps[half][:, 0:GRAM_HALF * FEATS].rearrange("p (g f) -> p g f", f=FEATS)
                    at = half * GRAM_HALF
                    dst = dots_buf[t % 2][:, :, at:at + GRAM_HALF].rearrange("p f g -> p g f")
                    nc.vector.tensor_copy(dst, src).then_inc(gram_out, 1)
                    halves_out += 1

            def rows(t):
                if t >= 1:
                    dve.wait_ge(cols_done, 2 * t)
                for fill in range(FILLS):
                    dve.wait_ge(rows_done, t * FILLS + fill + 1)
                    for i in row_share(0, fill):
                        dst, src = row_views(i)
                        last = nc.vector.tensor_copy(dst, src)
                    last.then_inc(rows_out[0], 1)

            def cols(t):
                dve.wait_ge(cols_done, 2 * t + 1)
                if t >= 1:
                    dve.wait_ge(layer1_done, 2 * t)
                for c in range(KC - 1):
                    dst, src = col_views(c)
                    last = nc.vector.tensor_copy(dst, src)
                last.then_inc(cols_out[0], 1)

            layer1_moved = 0

            def layer1_until(n):
                nonlocal layer1_moved
                t = layer1_moved
                if n < (t + 1) * N1:
                    return
                layer1_moved += 1
                dve.wait_ge(layer1_done, 2 * (t + 1))
                if t >= 1:
                    dve.wait_ge(layer2_done, 2 * t)
                for n in range(2):
                    last = nc.vector.tensor_scalar(h1[:, n + 2], layer1_ps[1][:, n * P:(n + 1) * P],
                                                   b1[:, n + 2:n + 3], 0.0, ALU.add, ALU.max)
                last.then_inc(layer1_out[1], 1)

            def layer2(t):
                dve.wait_ge(layer2_done, 2 * (t + 1))
                if t >= 1:
                    dve.wait_ge(y_done, t)
                nc.vector.tensor_scalar(h2[:, 1], layer2_ps[1][:, 0:P], b2[:, 1:2], 0.0,
                                        ALU.add, ALU.max).then_inc(layer2_out[1], 1)

            def layer3(t):
                dve.wait_ge(y_done, t + 1)
                nc.vector.tensor_copy(y_sb[:, t:t + 1], y_ps[:, 0:1]).then_inc(y_out, 1)

            steps = {"gram": gram_until, "rows": rows, "cols": cols, "layer1": layer1_until, "layer2": layer2,
                     "layer3": layer3}
            for step, n in ORDER:
                if step in steps:
                    steps[step](n)


def kernel(**inputs):
    import numpy as np
    import concourse.bacc as bacc
    from concourse.bass_utils import run_bass_kernel_spmd

    nc = bacc.Bacc("TRN2", target_bir_lowering=False, num_devices=1)
    arrays = {}

    def dram(name, array):
        array = np.ascontiguousarray(array)
        arrays[name] = array
        return nc.dram_tensor(name, array.shape, mybir.dt.from_np(array.dtype), kind="ExternalInput").ap()

    ids = np.asarray(inputs["ids"])
    ids_rows = dram("ids_rows", ids.reshape(TILES, P, TABLES).transpose(1, 0, 2))
    ids_cols = dram("ids_cols", ids[:, GATHERED:].T.reshape(1, PICKED, BATCH)).to_broadcast([P, PICKED, BATCH])
    dense = dram("dense", inputs["r_dense_features"]).rearrange("(t p) d -> p t d", p=P)
    tables = [dram(f"tbl_{i}", inputs[f"tbl_{i}"]) for i in range(TABLES)]

    w1 = dram("w1", inputs["W_top1"])
    w2 = dram("w2", inputs["W_top2"])
    small = dram("small", np.concatenate([
        np.asarray(inputs["b_top1"]).reshape(N1, P).T,
        np.asarray(inputs["b_top2"]).reshape(N2, P).T,
        np.asarray(inputs["W_top3"]).reshape(N2, P).T], axis=1))
    y = nc.dram_tensor("y", (P, TILES), F32, kind="ExternalOutput").ap()

    dlrm_program(nc, dense, ids_rows, ids_cols, tables, w1, w2, small, y)
    result = run_bass_kernel_spmd(nc, [arrays], core_ids=[0])
    return np.ascontiguousarray(result.results[0]["y"].T).reshape(BATCH, 1)
```

```python
from contextlib import ExitStack

import concourse.bass as bass
from concourse import mybir

F32 = mybir.dt.float32
F32R = mybir.dt.float32r
BF16 = mybir.dt.bfloat16
I32 = mybir.dt.int32
I16 = mybir.dt.int16
ALU = mybir.AluOpType
ACT = mybir.ActivationFunctionType

P = 128
BATCH = 512
EMB = 128
TABLES = 26
FEATS = TABLES + 1
SLOTS = 32
TILES = BATCH // P
LATE = TILES // 2
QUADS = P // SLOTS
GROUPS = P // QUADS

PICK_TABLES = [19, 20, 21, 22, 23, 24, 25, 18]
PICK_TILES = [0, 0, 0, 0, 0, 0, 0, 1]
PICKED = len(PICK_TABLES)
PICK_ROWS = 1000
EMB_TILES = 2
COL_RING = 2
RING = 2
CHUNKS = 8
SMALL_HOT = 4
PR = PICK_ROWS // CHUNKS
PR16 = PR // 16 * 16

TURN = 4


def feature_groups(tile):
    picked = {table + 1 for table, first in zip(PICK_TABLES, PICK_TILES) if tile >= first}
    groups = []
    for f in range(1, FEATS):
        if f in picked:
            continue
        if groups and groups[-1][1] == f and f - groups[-1][0] < TURN:
            groups[-1] = (groups[-1][0], f + 1)
        else:
            groups.append((f, f + 1))
    return groups


TURNS = [(t, f0, f1) for t in range(TILES) for f0, f1 in feature_groups(t)]
TURNED_BY = [sum(t <= tile for t, _, _ in TURNS) for tile in range(TILES)]
EMB_ROWS = max(f1 for _, _, f1 in TURNS) - 1

PAIR_AT = [i * (FEATS - 1) - i * (i - 1) // 2 for i in range(FEATS)]
PAIRS = FEATS * (FEATS - 1) // 2
KC = -(-PAIRS // P)
KLAST = PAIRS - (KC - 1) * P
WEIGHT_LOADS = 6
H1 = 512
H2 = 256
N1 = H1 // P
N2 = H2 // P
GRAM_HALF = GROUPS // 2
DOT_ROWS = P // GROUPS
BANK_ROWS = DOT_ROWS * QUADS
FILLS = -(-FEATS // BANK_ROWS)

ORDER = [
    ("hot", 0), ("dense", 0), ("hot", 1), ("pick", 0), ("hot", 2), ("turn", 1), ("pick", 1), ("hot", 3),
    ("turn", 2), ("pick", 2), ("hot", 4), ("turn", 3), ("pick", 3), ("hot", 5), ("turn", 4), ("pick", 4),
    ("hot", 6), ("turn", 5), ("pick", 5), ("turn", 6), ("hot", 7), ("pick", 6), ("turn", 7), ("turn", 8),
    ("gram", 2), ("weights", 0), ("gram", 4), ("pick", 7), ("turn", 10), ("rows", 0), ("gram", 5), ("turn", 11),
    ("cols", 0), ("gram", 6), ("layer1", 1), ("gram", 7), ("layer1", 2), ("turn", 12), ("gram", 8), ("layer1", 4),
    ("rows", 1), ("turn", 13), ("layer2", 2), ("cols", 1), ("layer3", 0), ("turn", 14), ("layer1", 5), ("turn", 15),
    ("layer1", 6), ("gram", 9), ("layer1", 7), ("gram", 10), ("layer1", 8), ("gram", 12),
    ("layer2", 3), ("rows", 2), ("layer2", 4), ("turn", 16), ("cols", 2), ("layer3", 1), ("turn", 17),
    ("layer1", 10), ("turn", 18), ("layer1", 11), ("turn", 20), ("layer1", 12), ("gram", 16),
    ("layer2", 5), ("rows", 3), ("layer2", 6), ("cols", 3), ("layer3", 2), ("layer1", 16), ("layer2", 8), ("layer3", 3),
]


def dlrm_program(nc, dense, ids_rows, ids_cols, tables, w1, w2, small, out):
    with ExitStack() as ctx:
        def sb(name, shape, dt):
            return ctx.enter_context(nc.sbuf_tensor(name, shape, dt))

        def bank(name):
            return ctx.enter_context(nc.psum_tensor(name, [P, 512], F32))

        def sem(name):
            return ctx.enter_context(nc.semaphore(name))

        row_ids = sb("row_ids", [P, TILES, TABLES], I32)
        col_ids = sb("col_ids", [P, COL_RING, BATCH], I32)
        col_ids16 = sb("col_ids16", [P, COL_RING, BATCH], I16)
        chunk_row = sb("chunk_row", [P, CHUNKS], I32)
        chunk_rows = sb("chunk_rows", [P, CHUNKS, BATCH], I16)
        dense_sb = sb("dense_sb", [P, TILES, EMB], F32)
        emb = sb("emb", [P, EMB_TILES, EMB_ROWS, EMB], F32)
        embT = sb("embT", [P, BATCH, SLOTS], F32)
        denseT = sb("denseT", [P, BATCH], F32)
        ident = sb("ident", [P, P], F32)
        ones = sb("ones", [P, P], F32)
        table = sb("table", [P, RING, CHUNKS, EMB], F32)
        table_hi = sb("table_hi", [P, 2, CHUNKS, EMB], F32R)
        table_lo = sb("table_lo", [P, 2, CHUNKS, EMB], F32R)
        small_hot = sb("small_hot", [P, SMALL_HOT, BATCH], BF16)
        one_hot = sb("one_hot", [P, 2, CHUNKS, BATCH], F32R)
        dots_buf = [sb("dots_even", [P, FEATS, GROUPS], F32), sb("dots_odd", [P, FEATS, GROUPS], F32)]
        pairs = sb("pairs", [GROUPS, QUADS, PAIRS], F32)
        pairsT = sb("pairsT", [P, KC, P], F32)
        w1_sb = sb("w1_sb", [P, KC + 2, H1], F32)
        w1_dense = sb("w1_dense", [P, H1], F32)
        w2_sb = sb("w2_sb", [P, N1, H2], F32)
        small_sb = sb("small_sb", [P, N1 + N2 + N2], F32)
        h1 = sb("h1", [P, N1, P], F32)
        h2 = sb("h2", [P, N2, P], F32)
        y_sb = sb("y_sb", [P, TILES], F32)
        b1 = small_sb[:, 0:N1]
        b2 = small_sb[:, N1:N1 + N2]
        w3 = small_sb[:, N1 + N2:N1 + 2 * N2]

        turn_ps = [bank("turn_ps0"), bank("turn_ps1")]
        pick_ps = [bank("pick_ps0"), bank("pick_ps1")]
        gram_ps = [bank("gram_ps0"), bank("gram_ps1")]
        row_ps = [bank("row_ps0"), bank("row_ps1")]
        layer1_ps = pick_ps
        layer2_ps = pick_ps
        y_ps = [pick_ps[0] if t < LATE else turn_ps[0] for t in range(TILES)]

        row_ids_in = sem("row_ids_in")
        col_ids_in = [sem(f"col_ids_in{j}") for j in range(PICKED)]
        dense_in = sem("dense_in")
        weights_in = sem("weights_in")
        table_in = [sem(f"table_in{j}") for j in range(PICKED)]
        rows_in = [sem(f"rows_in{x}") for x in range(len(TURNS))]
        out_stored = sem("out_stored")
        ones_set = sem("ones_set")
        ident_set = sem("ident_set")
        chunk_row_set = sem("chunk_row_set")
        chunk_rows_set = [sem("chunk_rows_set_act"), sem("chunk_rows_set_dve")]
        ids16_set = sem("ids16_set")
        pads_set = [sem("pads_set_dve"), sem("pads_set_pool")]
        w1_dense_set = sem("w1_dense_set")
        hi_set = sem("hi_set")
        lo_set = sem("lo_set")
        hot_set = sem("hot_set")
        small_hot_set = sem("small_hot_set")
        hot_widened = sem("hot_widened")
        picked = sem("picked")
        picked_out = sem("picked_out")
        dense_turned = sem("dense_turned")
        dense_out = sem("dense_out")
        turned = sem("turned")
        turned_out = sem("turned_out")
        gram_done = sem("gram_done")
        gram_out = sem("gram_out")
        rows_done = sem("rows_done")
        rows_out = [sem("rows_out_dve"), sem("rows_out_act")]
        cols_done = sem("cols_done")
        cols_out = [sem("cols_out_dve"), sem("cols_out_act")]
        layer1_done = sem("layer1_done")
        layer1_out = [sem("layer1_out_act"), sem("layer1_out_dve")]
        layer2_done = sem("layer2_done")
        layer2_out = [sem("layer2_out_act"), sem("layer2_out_dve")]
        y_done = sem("y_done")
        y_out = sem("y_out")

        def row_views(i):
            part, at = i % DOT_ROWS * GROUPS, i // DOT_ROWS % QUADS * P
            src = row_ps[i // BANK_ROWS % 2][part:part + GROUPS, at:at + P].rearrange("p (q f) -> p q f", q=QUADS)
            return pairs[:, :, PAIR_AT[i]:PAIR_AT[i] + FEATS - 1 - i], src[:, :, i + 1:FEATS]

        def row_share(engine, fill):
            rows = range(fill * BANK_ROWS, min((fill + 1) * BANK_ROWS, FEATS - 1))
            return [i for i in rows if i % DOT_ROWS * 2 // DOT_ROWS == engine]

        def col_views(c):
            k = P if c < KC - 1 else KLAST
            return pairsT[0:k, c], row_ps[c // 2][0:k, c % 2 * P:(c % 2 + 1) * P]

        def chunk_row_at(c0, c1):
            return chunk_row[:, c0:c1].rearrange("p (c o) -> p c o", o=1).to_broadcast([P, c1 - c0, BATCH])

        block = ctx.enter_context(nc.Block())

        @block.sync
        def _(sp):
            weight_loads = [
                (w1_sb[:, 0], w1[0:EMB]),
                (w1_sb[:, 1], w1[EMB + PAIRS:]),
                (w1_sb[:, 2:KC + 1], w1[EMB:EMB + (KC - 1) * P].rearrange("(c p) n -> p c n", p=P)),
                (w1_sb[0:KLAST, KC + 1], w1[EMB + (KC - 1) * P:EMB + PAIRS]),
                (w2_sb[:], w2.rearrange("(c p) n -> p c n", p=P)),
                (small_sb[:], small)]
            sp.dma_start(row_ids[:], ids_rows).then_inc(row_ids_in, 16)
            for j in range(PICKED):
                if j >= COL_RING:
                    sp.wait_ge(ids16_set, j - COL_RING + 1)
                s0 = PICK_TILES[j] * P
                sp.dma_start(col_ids[:, j % COL_RING, s0:], ids_cols[:, j, s0:]).then_inc(col_ids_in[j], 16)
                if j >= RING:
                    sp.wait_ge(lo_set, j - RING + 1)
                rows = tables[PICK_TABLES[j]].rearrange("(p c) d -> p c d", c=CHUNKS)
                sp.dma_start(table[0:PR16, j % RING], rows[0:PR16]).then_inc(table_in[j], 16)
                sp.dma_start(table[PR16:PR, j % RING], rows[PR16:PR]).then_inc(table_in[j], 16)
                if j == 0:
                    sp.dma_start(dense_sb[:], dense).then_inc(dense_in, 16)
                if 1 <= j <= len(weight_loads):
                    sp.dma_start(*weight_loads[j - 1]).then_inc(weights_in, 16)
            sp.wait_ge(y_out, TILES)
            sp.dma_start(out, y_sb[:]).then_inc(out_stored, 16)
            sp.wait_ge(out_stored, 16)

        @block.gpsimd
        def _(pool):
            nc.gpsimd.iota(chunk_row[:], [[1, CHUNKS]], base=0, channel_multiplier=CHUNKS).then_inc(chunk_row_set, 1)
            pool.wait_ge(ones_set, 1)
            nc.gpsimd.affine_select(out=ident[:], in_=ones[:], compare_op=ALU.is_equal, fill=0.0, base=0,
                                    pattern=[[-1, P]], channel_multiplier=1).then_inc(ident_set, 1)
            nc.gpsimd.memset(embT[:, BATCH // 2:BATCH, FEATS:SLOTS], 0.0).then_inc(pads_set[1], 1)
            pool.wait_ge(row_ids_in, 16)
            for x, (t, f0, f1) in enumerate(TURNS):
                if t >= EMB_TILES:
                    old = max(o for o, (tile, g0, g1) in enumerate(TURNS) if tile == t - EMB_TILES and g0 < f1)
                    pool.wait_ge(turned, old + 1)
                for f in range(f0, f1):
                    pool.indirect_dma_start(
                        emb[:, t % EMB_TILES, f - 1], None, tables[f - 1],
                        bass.IndirectOffsetOnAxis(ap=row_ids[:, t, f - 1:f], axis=0)).then_inc(rows_in[x], 16)

        @block.tensor
        def _(pe):
            turns_made = 0

            def turn_until(n):
                nonlocal turns_made
                while turns_made < n:
                    x = turns_made
                    t, f0, f1 = TURNS[x]
                    pe.wait_ge(rows_in[x], 16 * (f1 - f0))
                    if x >= 2:
                        pe.wait_ge(turned_out, x - 1)
                    elif x == 0:
                        pe.wait_ge(dense_out, 2)
                    for f in range(f0, f1):
                        mm = pe.transpose(turn_ps[x % 2][:, (f - f0) * P:(f - f0 + 1) * P],
                                          emb[:, t % EMB_TILES, f - 1], ident[:])
                    mm.then_inc(turned, 1)
                    turns_made += 1

            def turn_dense(_):
                pe.wait_ge(ident_set, 1)
                pe.wait_ge(dense_in, 16)
                for t in range(TILES):
                    mm = pe.transpose(turn_ps[0][:, t * P:(t + 1) * P], dense_sb[:, t], ident[:])
                mm.then_inc(dense_turned, 1)

            tables_picked = 0
            tiles_done = 0

            def pick(j):
                nonlocal tables_picked
                pe.wait_ge(hi_set, j + 1)
                pe.wait_ge(hot_set, j + 1)
                if j >= 2:
                    pe.wait_ge(picked_out, j - 1)
                if tiles_done >= 1:
                    pe.wait_ge(y_out, tiles_done)
                s0 = PICK_TILES[j] * P
                order = [*range(SMALL_HOT, CHUNKS), *range(SMALL_HOT)]
                for n, part in enumerate([table_hi, table_lo]):
                    if n == 1:
                        pe.wait_ge(lo_set, j + 1)
                    for c in order:
                        if n == 0 and c == 0:
                            pe.wait_ge(hot_widened, j + 1)
                        mm = pe.matmul(pick_ps[j % 2][:, s0:], part[0:PR, j % 2, c], one_hot[0:PR, j % 2, c, s0:],
                                       start=(n == 0 and c == order[0]), stop=(n == 1 and c == order[-1]))
                mm.then_inc(picked, 1)
                tables_picked += 1

            quarters_made = 0

            def gram_until(n):
                nonlocal quarters_made
                while quarters_made < n:
                    t, quarter = quarters_made // 4, quarters_made % 4
                    half = quarter // 2
                    if quarter == 0:
                        pe.wait_ge(turned_out, TURNED_BY[t])
                        pe.wait_ge(picked_out, sum(first <= t for first in PICK_TILES))
                        if t == 0:
                            pe.wait_ge(pads_set[0], 1)
                            pe.wait_ge(pads_set[1], 1)
                    if t >= 1 and quarter % 2 == 0:
                        pe.wait_ge(gram_out, 2 * (t - 1) + half + 1)
                    for g in range(quarter * GROUPS // 4, (quarter + 1) * GROUPS // 4):
                        at = g % GRAM_HALF * FEATS
                        for q in range(QUADS):
                            b = t * P + q * GROUPS + g
                            mm = pe.matmul(gram_ps[half][q * SLOTS:(q + 1) * SLOTS, at:at + FEATS],
                                           embT[:, b, :], embT[:, b, 0:FEATS], start=True, stop=True,
                                           tile_position=(0, q * SLOTS))
                    if quarter % 2 == 1:
                        mm.then_inc(gram_done, 1)
                    quarters_made += 1

            def rows(t):
                pe.wait_ge(gram_out, 2 * (t + 1))
                if t >= 1:
                    pe.wait_ge(cols_out[0], t)
                    pe.wait_ge(cols_out[1], t)
                dots = dots_buf[t % 2]
                for fill in range(FILLS):
                    if fill >= 2:
                        pe.wait_ge(rows_out[0], t * FILLS + fill - 1)
                        pe.wait_ge(rows_out[1], t * FILLS + fill - 1)
                    for n, i in enumerate(range(fill * BANK_ROWS, min((fill + 1) * BANK_ROWS, FEATS), DOT_ROWS)):
                        src = dots[:, i:min(i + DOT_ROWS, FEATS)].rearrange("p r g -> p (r g)")
                        mm = pe.transpose(row_ps[fill % 2][0:src.shape[1], n * P:(n + 1) * P], src, ident[:])
                    mm.then_inc(rows_done, 1)

            def cols(t):
                pe.wait_ge(rows_out[0], (t + 1) * FILLS)
                pe.wait_ge(rows_out[1], (t + 1) * FILLS)
                for c in range(KC):
                    k = P if c < KC - 1 else KLAST
                    for q in range(QUADS):
                        at = c % 2 * P + q * GROUPS
                        mm = pe.transpose(row_ps[c // 2][0:k, at:at + GROUPS], pairs[:, q, c * P:c * P + k],
                                          ident[0:GROUPS, 0:GROUPS])
                    if c != 0:
                        mm.then_inc(cols_done, 1)

            blocks_made = 0

            def layer1_until(n):
                nonlocal blocks_made
                while blocks_made < n:
                    t, block_of = blocks_made // N1, blocks_made % N1
                    if block_of == 0 and t == 0:
                        pe.wait_ge(w1_dense_set, 1)
                    if block_of == 0:
                        pe.wait_ge(picked_out, tables_picked)
                    if block_of == 0 and t >= 1:
                        pe.wait_ge(layer2_out[0], t)
                        pe.wait_ge(layer2_out[1], t)
                        pe.wait_ge(y_out, min(t, LATE))
                    dst = layer1_ps[block_of // 2][:, block_of % 2 * P:(block_of % 2 + 1) * P]
                    at = slice(block_of * P, (block_of + 1) * P)
                    pe.matmul(dst, w1_dense[:, at], denseT[:, t * P:(t + 1) * P], start=True, stop=False)
                    if block_of == 0:
                        pe.wait_ge(cols_out[0], t + 1)
                        pe.wait_ge(cols_out[1], t + 1)
                    for c in range(KC):
                        k = P if c < KC - 1 else KLAST
                        mm = pe.matmul(dst, w1_sb[0:k, 2 + c, at], pairsT[0:k, c], start=False, stop=(c == KC - 1))
                    if block_of % 2 == 1:
                        mm.then_inc(layer1_done, 1)
                    blocks_made += 1

            blocks2_made = 0

            def layer2_until(n):
                nonlocal blocks2_made
                while blocks2_made < n:
                    t, block_of = blocks2_made // N2, blocks2_made % N2
                    for c in range(N1):
                        if block_of == 0 and c % 2 == 0:
                            pe.wait_ge(layer1_out[c // 2], t + 1)
                        mm = pe.matmul(layer2_ps[block_of][:, 0:P], w2_sb[:, c, block_of * P:(block_of + 1) * P],
                                       h1[:, c], start=(c == 0), stop=(c == N1 - 1))
                    mm.then_inc(layer2_done, 1)
                    blocks2_made += 1

            def layer3(t):
                nonlocal tiles_done
                pe.wait_ge(layer2_out[0], t + 1)
                pe.wait_ge(layer2_out[1], t + 1)
                if t >= LATE:
                    pe.wait_ge(turned_out, len(TURNS))
                    pe.wait_ge(y_out, t)
                for c in range(N2):
                    mm = pe.matmul(y_ps[t][:, 0:1], h2[:, c], w3[:, c:c + 1], start=(c == 0), stop=(c == N2 - 1))
                mm.then_inc(y_done, 1)
                tiles_done += 1

            steps = {"dense": turn_dense, "pick": pick, "turn": turn_until, "gram": gram_until, "rows": rows,
                     "cols": cols, "layer1": layer1_until, "layer2": layer2_until, "layer3": layer3}
            for step, n in ORDER:
                if step in steps:
                    steps[step](n)

        @block.scalar
        def _(act):
            turns_out = 0

            def turn_until(n):
                nonlocal turns_out
                while turns_out < n:
                    x = turns_out
                    t, f0, f1 = TURNS[x]
                    src = turn_ps[x % 2][:, 0:(f1 - f0) * P].rearrange("p (f b) -> p f b", f=f1 - f0)
                    act.wait_ge(turned, x + 1)
                    nc.scalar.copy(embT[:, t * P:(t + 1) * P, f0:f1].rearrange("p b f -> p f b"),
                                   src).then_inc(turned_out, 1)
                    turns_out += 1

            def round_table(j):
                act.wait_ge(table_in[j], 32)
                if j >= 2:
                    act.wait_ge(picked, j - 1)
                nc.scalar.copy(table_hi[0:PR, j % 2], table[0:PR, j % RING]).then_inc(hi_set, 1)

            def narrow_ids(j):
                act.wait_ge(col_ids_in[j], 16)
                if j >= COL_RING:
                    act.wait_ge(hot_set, j - COL_RING + 1)
                s0 = PICK_TILES[j] * P
                nc.scalar.copy(col_ids16[:, j % COL_RING, s0:], col_ids[:, j % COL_RING, s0:]).then_inc(ids16_set, 1)

            def widen_hot(j):
                act.wait_ge(small_hot_set, j + 1)
                if j >= 2:
                    act.wait_ge(picked, j - 1)
                s0 = PICK_TILES[j] * P
                nc.scalar.copy(one_hot[0:PR, j % 2, 0:SMALL_HOT, s0:], small_hot[0:PR, :, s0:]).then_inc(hot_widened, 1)

            def move_dense(_):
                act.wait_ge(dense_turned, 1)
                nc.scalar.copy(denseT[:], turn_ps[0][:]).then_inc(dense_out, 1)
                nc.scalar.copy(embT[:, :, 0], turn_ps[0][:]).then_inc(dense_out, 1)

            def hot(j):
                round_table(j)
                widen_hot(j)
                if j + 1 < PICKED:
                    narrow_ids(j + 1)

            def pick(j):
                act.wait_ge(picked, j + 1)
                s0 = PICK_TILES[j] * P
                nc.scalar.copy(embT[:, s0:, PICK_TABLES[j] + 1], pick_ps[j % 2][:, s0:]).then_inc(picked_out, 1)

            def rows(t):
                if t >= 1:
                    act.wait_ge(cols_done, 2 * t)
                for fill in range(FILLS):
                    act.wait_ge(rows_done, t * FILLS + fill + 1)
                    for i in row_share(1, fill):
                        dst, src = row_views(i)
                        last = nc.scalar.copy(dst, src)
                    last.then_inc(rows_out[1], 1)

            def cols(t):
                act.wait_ge(cols_done, 2 * (t + 1))
                if t >= 1:
                    act.wait_ge(layer1_done, 2 * t)
                dst, src = col_views(KC - 1)
                nc.scalar.copy(dst, src).then_inc(cols_out[1], 1)

            layer1_moved = 0

            def layer1_until(n):
                nonlocal layer1_moved
                t = layer1_moved
                if n < t * N1 + N1 // 2:
                    return
                layer1_moved += 1
                if t == 0:
                    act.wait_ge(weights_in, 16 * WEIGHT_LOADS)
                act.wait_ge(layer1_done, 2 * t + 1)
                if t >= 1:
                    act.wait_ge(layer2_done, 2 * t)
                for n in range(2):
                    last = nc.scalar.activation(h1[:, n], layer1_ps[0][:, n * P:(n + 1) * P], ACT.Relu,
                                                bias=b1[:, n:n + 1])
                last.then_inc(layer1_out[0], 1)

            layer2_moved = 0

            def layer2_until(n):
                nonlocal layer2_moved
                t = layer2_moved
                if n < t * N2 + 1:
                    return
                layer2_moved += 1
                act.wait_ge(layer2_done, 2 * t + 1)
                if t >= 1:
                    act.wait_ge(y_done, t)
                nc.scalar.activation(h2[:, 0], layer2_ps[0][:, 0:P], ACT.Relu,
                                     bias=b2[:, 0:1]).then_inc(layer2_out[0], 1)

            act.wait_ge(chunk_row_set, 1)
            nc.scalar.copy(chunk_rows[:, 0:SMALL_HOT], chunk_row_at(0, SMALL_HOT)).then_inc(chunk_rows_set[0], 1)
            narrow_ids(0)
            steps = {"dense": move_dense, "hot": hot, "pick": pick, "turn": turn_until, "rows": rows, "cols": cols,
                     "layer1": layer1_until, "layer2": layer2_until}
            for step, n in ORDER:
                if step in steps:
                    steps[step](n)

        @block.vector
        def _(dve):
            nc.vector.memset(ones[:], 1.0).then_inc(ones_set, 1)
            nc.vector.memset(embT[:, 0:BATCH // 2, FEATS:SLOTS], 0.0).then_inc(pads_set[0], 1)
            dve.wait_ge(chunk_row_set, 1)
            nc.vector.tensor_copy(chunk_rows[:, SMALL_HOT:CHUNKS],
                                  chunk_row_at(SMALL_HOT, CHUNKS)).then_inc(chunk_rows_set[1], 1)
            dve.wait_ge(chunk_rows_set[0], 1)
            dve.wait_ge(chunk_rows_set[1], 1)

            def hot(j):
                s0 = PICK_TILES[j] * P
                ids = col_ids16[0:PR, j % COL_RING:j % COL_RING + 1, s0:]
                dve.wait_ge(ids16_set, j + 1)
                if j >= 1:
                    dve.wait_ge(hot_widened, j)
                nc.vector.tensor_tensor(small_hot[0:PR, :, s0:], chunk_rows[0:PR, 0:SMALL_HOT, s0:],
                                        ids.to_broadcast([PR, SMALL_HOT, BATCH - s0]),
                                        ALU.is_equal).then_inc(small_hot_set, 1)
                if j >= 2:
                    dve.wait_ge(picked, j - 1)
                nc.vector.tensor_tensor(one_hot[0:PR, j % 2, SMALL_HOT:CHUNKS, s0:],
                                        chunk_rows[0:PR, SMALL_HOT:CHUNKS, s0:],
                                        ids.to_broadcast([PR, CHUNKS - SMALL_HOT, BATCH - s0]),
                                        ALU.is_equal).then_inc(hot_set, 1)
                dve.wait_ge(hi_set, j + 1)
                nc.vector.tensor_tensor(table_lo[0:PR, j % 2], table[0:PR, j % RING],
                                        table_hi[0:PR, j % 2].bitcast(F32), ALU.subtract).then_inc(lo_set, 1)

            def weights(_):
                dve.wait_ge(weights_in, 16 * WEIGHT_LOADS)
                nc.vector.tensor_tensor(w1_dense[:], w1_sb[:, 0], w1_sb[:, 1], ALU.add).then_inc(w1_dense_set, 1)

            halves_out = 0

            def gram_until(quarters):
                nonlocal halves_out
                while halves_out < quarters // 2:
                    t, half = halves_out // 2, halves_out % 2
                    dve.wait_ge(gram_done, halves_out + 1)
                    if t >= 2:
                        dve.wait_ge(rows_done, (t - 1) * FILLS)
                    src = gram_ps[half][:, 0:GRAM_HALF * FEATS].rearrange("p (g f) -> p g f", f=FEATS)
                    at = half * GRAM_HALF
                    dst = dots_buf[t % 2][:, :, at:at + GRAM_HALF].rearrange("p f g -> p g f")
                    nc.vector.tensor_copy(dst, src).then_inc(gram_out, 1)
                    halves_out += 1

            def rows(t):
                if t >= 1:
                    dve.wait_ge(cols_done, 2 * t)
                for fill in range(FILLS):
                    dve.wait_ge(rows_done, t * FILLS + fill + 1)
                    for i in row_share(0, fill):
                        dst, src = row_views(i)
                        last = nc.vector.tensor_copy(dst, src)
                    last.then_inc(rows_out[0], 1)

            def cols(t):
                dve.wait_ge(cols_done, 2 * t + 1)
                if t >= 1:
                    dve.wait_ge(layer1_done, 2 * t)
                for c in range(KC - 1):
                    dst, src = col_views(c)
                    last = nc.vector.tensor_copy(dst, src)
                last.then_inc(cols_out[0], 1)

            layer1_moved = 0

            def layer1_until(n):
                nonlocal layer1_moved
                t = layer1_moved
                if n < (t + 1) * N1:
                    return
                layer1_moved += 1
                dve.wait_ge(layer1_done, 2 * (t + 1))
                if t >= 1:
                    dve.wait_ge(layer2_done, 2 * t)
                for n in range(2):
                    last = nc.vector.tensor_scalar(h1[:, n + 2], layer1_ps[1][:, n * P:(n + 1) * P],
                                                   b1[:, n + 2:n + 3], 0.0, ALU.add, ALU.max)
                last.then_inc(layer1_out[1], 1)

            layer2_moved = 0

            def layer2_until(n):
                nonlocal layer2_moved
                t = layer2_moved
                if n < (t + 1) * N2:
                    return
                layer2_moved += 1
                dve.wait_ge(layer2_done, 2 * (t + 1))
                if t >= 1:
                    dve.wait_ge(y_done, t)
                nc.vector.tensor_scalar(h2[:, 1], layer2_ps[1][:, 0:P], b2[:, 1:2], 0.0,
                                        ALU.add, ALU.max).then_inc(layer2_out[1], 1)

            def layer3(t):
                dve.wait_ge(y_done, t + 1)
                nc.vector.tensor_copy(y_sb[:, t:t + 1], y_ps[t][:, 0:1]).then_inc(y_out, 1)

            steps = {"hot": hot, "weights": weights, "gram": gram_until, "rows": rows, "cols": cols,
                     "layer1": layer1_until, "layer2": layer2_until, "layer3": layer3}
            for step, n in ORDER:
                if step in steps:
                    steps[step](n)


def kernel(**inputs):
    import numpy as np
    import concourse.bacc as bacc
    from concourse.bass_utils import run_bass_kernel_spmd

    nc = bacc.Bacc("TRN2", target_bir_lowering=False, num_devices=1)
    arrays = {}

    def dram(name, array):
        array = np.ascontiguousarray(array)
        arrays[name] = array
        return nc.dram_tensor(name, array.shape, mybir.dt.from_np(array.dtype), kind="ExternalInput").ap()

    ids = np.asarray(inputs["ids"])
    ids_rows = dram("ids_rows", ids.reshape(TILES, P, TABLES).transpose(1, 0, 2))
    ids_cols = dram("ids_cols", ids[:, PICK_TABLES].T.reshape(1, PICKED, BATCH)).to_broadcast([P, PICKED, BATCH])
    dense = dram("dense", inputs["r_dense_features"]).rearrange("(t p) d -> p t d", p=P)
    tables = [dram(f"tbl_{i}", inputs[f"tbl_{i}"]) for i in range(TABLES)]

    w1 = dram("w1", inputs["W_top1"])
    w2 = dram("w2", inputs["W_top2"])
    small = dram("small", np.concatenate([
        np.asarray(inputs["b_top1"]).reshape(N1, P).T,
        np.asarray(inputs["b_top2"]).reshape(N2, P).T,
        np.asarray(inputs["W_top3"]).reshape(N2, P).T], axis=1))
    y = nc.dram_tensor("y", (P, TILES), F32, kind="ExternalOutput").ap()

    dlrm_program(nc, dense, ids_rows, ids_cols, tables, w1, w2, small, y)
    result = run_bass_kernel_spmd(nc, [arrays], core_ids=[0])
    return np.ascontiguousarray(result.results[0]["y"].T).reshape(BATCH, 1)
```
